# Optimizing a Trainium2 kernel written in Bass

```python
import numpy as np
import jax
import jax.numpy as jnp

def _softmax(x, axis=-1):
    return jax.nn.softmax(x, axis=axis)

def _gelu(x):
    return jax.nn.gelu(x, approximate=True)

def _silu(x):
    return jax.nn.silu(x)

def _sigmoid(x):
    return jax.nn.sigmoid(x)

def _layernorm(x, axis=-1, eps=1e-05):
    m = jnp.mean(x, axis=axis, keepdims=True)
    v = jnp.var(x, axis=axis, keepdims=True)
    return (x - m) / jnp.sqrt(v + eps)

def _scatter_add(tgt, idx, src, axis=0):
    return tgt.at[idx].add(src)

def _segment_sum(src, seg, n):
    return jax.ops.segment_sum(src, seg, n)
kernel_name = 'mk_cond_resid_d1_seqx_r4_9310d2'

def setup_inputs(seed: int=0):
    np.random.seed(seed)
    _w = jnp.asarray

    def _rec_inputs():
        import jax
        import jax.numpy as jnp
        _rk = jax.random.key(seed)
        x = -5.722e-05 + 0.9998 * jax.random.normal(jax.random.fold_in(_rk, 1), (8, 256, 256), jnp.float32)
        _lenS = 256 - jax.random.randint(jax.random.fold_in(_rk, 7), (8,), 0, max(1, 256 // 4) + 1, jnp.int32)
        _lenS2 = 256 - jax.random.randint(jax.random.fold_in(_rk, 8), (8,), 0, max(1, 256 // 4) + 1, jnp.int32)
        cond_1024 = -0.0142567 + 1.00875 * jax.random.normal(jax.random.fold_in(_rk, 11), (8, 256), jnp.float32)
        return (x, cond_1024)
    x, cond_1024 = _rec_inputs()

    def _L0_cond_setup():
        import jax, jax.numpy as jnp
        import numpy as np
        MODEL_DIM = 256
        NUM_HEADS = 16
        HEAD_DIM = MODEL_DIM // NUM_HEADS
        BATCH = 16
        KEY_LEN = 1024
        key = jax.random.key(seed)
        ks = jax.random.split(key, 10)
        u = lambda k, shape: jax.random.uniform(k, shape, jnp.float32, -0.5, 0.5)
        return {'hidden_states': jax.random.normal(ks[0], (BATCH, 1, MODEL_DIM), jnp.float32), 'key_value_states': jax.random.normal(ks[1], (BATCH, KEY_LEN, MODEL_DIM), jnp.float32), 'Wq': u(ks[2], (MODEL_DIM, MODEL_DIM)), 'bq': u(ks[3], (MODEL_DIM,)), 'Wk': u(ks[4], (MODEL_DIM, MODEL_DIM)), 'bk': u(ks[5], (MODEL_DIM,)), 'Wv': u(ks[6], (MODEL_DIM, MODEL_DIM)), 'bv': u(ks[7], (MODEL_DIM,)), 'Wo': u(ks[8], (MODEL_DIM, MODEL_DIM)), 'bo': u(ks[9], (MODEL_DIM,))}
    _L0_cond_all = _L0_cond_setup()
    _L0_cond_in = {k: v for k, v in _L0_cond_all.items() if k in ('Wq', 'bq', 'Wk', 'bk', 'Wv', 'bv', 'Wo', 'bo')}
    del _L0_cond_all
    return {'x': x, 'cond_1024': cond_1024, 'L0_cond_Wq': _L0_cond_in['Wq'], 'L0_cond_bq': _L0_cond_in['bq'], 'L0_cond_Wk': _L0_cond_in['Wk'], 'L0_cond_bk': _L0_cond_in['bk'], 'L0_cond_Wv': _L0_cond_in['Wv'], 'L0_cond_bv': _L0_cond_in['bv'], 'L0_cond_Wo': _L0_cond_in['Wo'], 'L0_cond_bo': _L0_cond_in['bo']}

def reference(x, cond_1024, L0_cond_Wq, L0_cond_bq, L0_cond_Wk, L0_cond_bk, L0_cond_Wv, L0_cond_bv, L0_cond_Wo, L0_cond_bo):
    import jax
    import jax.numpy as jnp

    def _L0_cond_ref(hidden_states, key_value_states, Wq, bq, Wk, bk, Wv, bv, Wo, bo):
        import jax, jax.numpy as jnp
        import numpy as np
        MODEL_DIM = 256
        NUM_HEADS = 16
        HEAD_DIM = MODEL_DIM // NUM_HEADS
        BATCH = 16
        KEY_LEN = 1024
        B, K = (key_value_states.shape[0], key_value_states.shape[1])
        H, Dh = (NUM_HEADS, HEAD_DIM)
        q = hidden_states @ Wq.T + bq
        k = key_value_states @ Wk.T + bk
        v = key_value_states @ Wv.T + bv
        q = q.reshape(B, 1, H, Dh).transpose(0, 2, 1, 3)
        k = k.reshape(B, K, H, Dh).transpose(0, 2, 1, 3)
        v = v.reshape(B, K, H, Dh).transpose(0, 2, 1, 3)
        q = q / jnp.sqrt(jnp.asarray(Dh, q.dtype))
        scores = jnp.einsum('bhqd,bhkd->bhqk', q, k)[:, :, 0, :]
        attn = jnp.clip(scores, 0.0, 1.0)
        context = attn[..., None] * v
        context = context.transpose(0, 2, 1, 3).reshape(B, K, H * Dh)
        output = context @ Wo.T + bo
        return output
    x = x + _L0_cond_ref(cond_1024[:, None, :], x, L0_cond_Wq, L0_cond_bq, L0_cond_Wk, L0_cond_bk, L0_cond_Wv, L0_cond_bv, L0_cond_Wo, L0_cond_bo)
    return x

_drawn_inputs = setup_inputs


def setup_inputs(seed=0):
    import zlib

    import numpy as np

    out = dict(_drawn_inputs(seed))
    spreads = {}
    factors = {'L0_cond_bo': 2.819}
    for name, (base, spread) in spreads.items():
        noise = np.random.default_rng([zlib.crc32(name.encode()), seed]).standard_normal(out[name].shape)
        drawn = base * np.exp(spread * noise) if base else spread * noise
        out[name] = jnp.asarray(drawn.astype(out[name].dtype))
    for name, factor in factors.items():
        out[name] = (out[name] * factor).astype(out[name].dtype)
    return out
```

```python
from contextlib import ExitStack

import concourse.bass as bass
from concourse import mybir

F32 = mybir.dt.float32
F32R = mybir.dt.float32r
BF16 = mybir.dt.bfloat16
ALU = mybir.AluOpType
ACT = mybir.ActivationFunctionType

P = 128
B, T, D = 8, 256, 256
HEADS, HEAD = 16, 16
K = D // P
N = 512
CHUNKS = B * T // N
BPC = N // T
PAIRS = CHUNKS // 2
HPK = HEADS // K
Q = 32
SLOT = 160
WARM = 9

BQ, BK, BV, BO = 0, K, 2 * K, 3 * K
ONE_HOT = 4 * K
IN_HEAD = ONE_HOT + 2 * HEADS
SMALL = IN_HEAD + HPK


def build(nc, x_t, wq_cond, wk, wv, wo, small, y_t):
    with ExitStack() as ctx:
        def sb(name, shape, dt=F32):
            return ctx.enter_context(nc.sbuf_tensor(name, shape, dt))

        def bank(name):
            return ctx.enter_context(nc.psum_tensor(name, [P, N], F32))

        def sem(name):
            return ctx.enter_context(nc.semaphore(name))

        x_s = sb("x_s", [P, CHUNKS, K, N])
        x_h = sb("x_h", [P, CHUNKS, K, N], F32R)
        x_l = sb("x_l", [P, CHUNKS, K, N], F32R)
        v_s = sb("v_s", [P, CHUNKS, K, N])
        ctx_s = sb("ctx_s", [P, CHUNKS, K, N])
        ctx_h = sb("ctx_h", [P, CHUNKS, K, N], F32R)
        ctx_l = sb("ctx_l", [P, CHUNKS, K, N], F32R)
        y_s = sb("y_s", [P, CHUNKS, K, N])
        wqc_s = sb("wqc_s", [P, K, D + B])
        wk_s = sb("wk_s", [P, K, D])
        wv_s = sb("wv_s", [P, K, D])
        wv_h = sb("wv_h", [P, K, D], F32R)
        wv_l = sb("wv_l", [P, K, D], F32R)
        wo_s = sb("wo_s", [P, K, D])
        wo_h = sb("wo_h", [P, K, D], F32R)
        wo_l = sb("wo_l", [P, K, D], F32R)
        small_s = sb("small_s", [P, SMALL])
        q_s = sb("q_s", [P, K, B])
        q_heads = sb("q_heads", [P, K, B, HPK])
        bk_heads = sb("bk_heads", [P, K, P])
        a_st = sb("a_st", [P, K, B, SLOT], F32R)
        a_flat = a_st[:].rearrange("p k b s -> p k (b s)")
        score_bias = sb("score_bias", [P, PAIRS, BPC])
        low_s = sb("low_s", [P, N])
        sum_s = sb("sum_s", [P, N])
        clip_s = sb("clip_s", [P, N])
        attn = sb("attn", [P, PAIRS, N], F32R)
        spread = sb("spread", [P, 2, K, P], F32R)
        zeros = sb("zeros", [P, N], BF16)
        act_warm = sb("act_warm", [P, 1])

        v_ps = [bank(f"v_ps{i}") for i in range(2)]
        e_ps = [bank(f"e_ps{i}") for i in range(2)]
        o_ps = [bank(f"o_ps{i}") for i in range(2)]
        s_ps = bank("s_ps")
        p_ps = bank("p_ps")
        q_ps = p_ps[:, 0:K * B].rearrange("p (k b) -> p k b", k=K)
        cb_ps = p_ps[:, 16:16 + B].rearrange("p (r c b) -> p r c b", r=PAIRS, c=2)
        a_ps = p_ps[:, 256:512].rearrange("p (k b h) -> p k b h", k=K, b=B)

        x_in = [[sem(f"x_in{c}_{k}") for k in range(K)] for c in range(CHUNKS)]
        wqc_in, wk_in, wv_in, wo_in, small_in = (sem(s) for s in ("wqc_in", "wk_in", "wv_in", "wo_in", "small_in"))
        zeros_set = sem("zeros_set")
        a_zeroed = sem("a_zeroed")
        bk_zeroed = sem("bk_zeroed")
        bk_set = sem("bk_set")
        wv_high, wv_low, wo_high, wo_low = (sem(s) for s in ("wv_high", "wv_low", "wo_high", "wo_low"))
        xh_done = sem("xh_done")
        xl_done = sem("xl_done")
        xl_pool = sem("xl_pool")
        q_made, q_biased, q_spread = (sem(s) for s in ("q_made", "q_biased", "q_spread"))
        a_made, a_high, a_low = (sem(s) for s in ("a_made", "a_high", "a_low"))
        cb_set = sem("cb_set")
        spread_set = sem("spread_set")
        v_made, v_kept = sem("v_made"), sem("v_kept")
        s_made, s_low, s_sum, s_clip = (sem(s) for s in ("s_made", "s_low", "s_sum", "s_clip"))
        attn_high, attn_low = sem("attn_high"), sem("attn_low")
        e_made = sem("e_made")
        ctx_made, ctx_high, ctx_low = (sem(s) for s in ("ctx_made", "ctx_high", "ctx_low"))
        o_made, y_made, y_out = sem("o_made"), sem("y_made"), sem("y_out")

        tiles = [(c, k) for c in range(CHUNKS) for k in range(K)]
        DVE_XL = 2

        def bias(at, k):
            return small_s[:, at + k:at + k + 1]

        block = ctx.enter_context(nc.Block())

        @block.sync
        def _(sp):
            sp.dma_start(wv_s[:], wv).then_inc(wv_in, 16)
            for k in range(K):
                sp.dma_start(x_s[:, 0, k, :], x_t[0, :, k, :]).then_inc(x_in[0][k], 16)
            sp.dma_start(wqc_s[:], wq_cond).then_inc(wqc_in, 16)
            sp.dma_start(small_s[:], small).then_inc(small_in, 16)
            for k in range(K):
                sp.dma_start(x_s[:, 1, k, :], x_t[1, :, k, :]).then_inc(x_in[1][k], 16)
            sp.dma_start(wk_s[:], wk).then_inc(wk_in, 16)
            sp.dma_start(x_s[:, 2], x_t[2]).then_inc(x_in[2][0], 16)
            sp.dma_start(x_s[:, 3], x_t[3]).then_inc(x_in[3][0], 16)
            sp.dma_start(wo_s[:], wo).then_inc(wo_in, 16)
            for i, (c, k) in enumerate(tiles):
                sp.wait_ge(y_made, i + 1)
                sp.dma_start(y_t[c, k], y_s[:, c, k, :]).then_inc(y_out, 16)
            sp.wait_ge(y_out, 16 * len(tiles))

        @block.gpsimd
        def _(pool):
            pool.memset(a_st[:].bitcast(F32), 0.0).then_inc(a_zeroed, 1)
            pool.memset(bk_heads[:], 0.0).then_inc(bk_zeroed, 1)
            pool.wait_ge(bk_zeroed, 1)
            pool.wait_ge(small_in, 16)
            for k in range(K):
                for par in range(2):
                    at = 2 * Q + par * Q + k * HPK
                    pool.tensor_scalar(bk_heads[:, k, at:at + HPK], small_s[:, IN_HEAD:IN_HEAD + HPK],
                                       bias(BK, k), float(HEAD) ** -0.5, ALU.mult, ALU.mult).then_inc(bk_set, 1)
            for c in range(DVE_XL, CHUNKS):
                pool.wait_ge(xh_done, K * (c + 1))
                pool.tensor_tensor(x_l[:, c], x_s[:, c], x_h[:, c].bitcast(F32), ALU.subtract).then_inc(xl_pool, 1)

        @block.scalar
        def _(act):
            def x_high(c):
                for k in range(K):
                    if c < 2 or k == 0:
                        act.wait_ge(x_in[c][k], 16)
                    act.copy(x_h[:, c, k, :], x_s[:, c, k, :]).then_inc(xh_done, 1)

            def keep_v(c):
                for k in range(K):
                    act.wait_ge(v_made, K * c + k + 1)
                    act.activation(v_s[:, c, k, :], v_ps[k][:], ACT.Identity, bias=bias(BV, k)).then_inc(v_kept, 1)

            def score_low(r):
                act.wait_ge(s_made, r + 1)
                if r == 0:
                    act.wait_ge(cb_set, 2)
                else:
                    act.wait_ge(s_sum, r)
                for j in range(BPC):
                    act.activation(low_s[2 * Q:, j * T:(j + 1) * T], s_ps[2 * Q:, j * T:(j + 1) * T], ACT.Identity,
                                   bias=score_bias[2 * Q:, r, j:j + 1]).then_inc(s_low, 1)

            def ctx_round(c):
                for k in range(K):
                    act.wait_ge(ctx_made, K * c + k + 1)
                    act.copy(ctx_h[:, c, k, :], ctx_s[:, c, k, :]).then_inc(ctx_high, 1)

            act.wait_ge(zeros_set, 1)
            act.activation(act_warm[:], zeros[:, 0:1], ACT.Identity)
            x_high(0)
            x_high(1)
            act.wait_ge(small_in, 16)
            keep_v(0)
            x_high(2)
            keep_v(1)
            x_high(3)
            score_low(0)
            act.wait_ge(wo_in, 16)
            act.copy(wo_h[:], wo_s[:]).then_inc(wo_high, 1)
            keep_v(2)
            ctx_round(0)
            score_low(1)
            keep_v(3)
            for c in range(1, CHUNKS):
                ctx_round(c)

        @block.vector
        def _(dve):
            def x_low(c):
                for k in range(K):
                    dve.wait_ge(xh_done, K * c + k + 1)
                    dve.tensor_tensor(x_l[:, c, k, :], x_s[:, c, k, :], x_h[:, c, k, :].bitcast(F32),
                                      ALU.subtract).then_inc(xl_done, 1)

            def attention(r):
                half = slice(0, 2 * Q)
                dve.wait_ge(s_low, BPC * (r + 1))
                dve.tensor_tensor(sum_s[half], s_ps[half], low_s[2 * Q:], ALU.add).then_inc(s_sum, 1)
                dve.wait_ge(s_sum, r + 1)
                dve.tensor_scalar(clip_s[half], sum_s[half], 0.0, 1.0, ALU.max, ALU.min).then_inc(s_clip, 1)
                dve.wait_ge(s_clip, r + 1)
                dve.tensor_copy(attn[half, r, :], clip_s[half]).then_inc(attn_high, 1)
                dve.wait_ge(attn_high, r + 1)
                dve.tensor_tensor(attn[2 * Q:, r, :], clip_s[half], attn[half, r, :].bitcast(F32),
                                  ALU.subtract).then_inc(attn_low, 1)

            def context(c):
                for k in range(K):
                    dve.wait_ge(e_made, K * c + k + 1)
                    dve.wait_ge(v_kept, K * c + k + 1)
                    dve.tensor_tensor(ctx_s[:, c, k, :], e_ps[k][:], v_s[:, c, k, :], ALU.mult).then_inc(ctx_made, 1)
                for k in range(K):
                    dve.wait_ge(ctx_high, K * c + k + 1)
                    dve.tensor_tensor(ctx_l[:, c, k, :], ctx_s[:, c, k, :], ctx_h[:, c, k, :].bitcast(F32),
                                      ALU.subtract).then_inc(ctx_low, 1)

            def output(c):
                for k in range(K):
                    dve.wait_ge(o_made, K * c + k + 1)
                    dve.scalar_tensor_tensor(y_s[:, c, k, :], o_ps[k][:], bias(BO, k), x_s[:, c, k, :],
                                             ALU.add, ALU.add).then_inc(y_made, 1)

            dve.memset(zeros[:], 0.0).then_inc(zeros_set, 1)
            dve.wait_ge(wv_in, 16)
            dve.tensor_copy(wv_h[:], wv_s[:]).then_inc(wv_high, 1)
            dve.wait_ge(wv_high, 1)
            dve.tensor_tensor(wv_l[:], wv_s[:], wv_h[:].bitcast(F32), ALU.subtract).then_inc(wv_low, 1)
            x_low(0)
            dve.wait_ge(small_in, 16)
            dve.tensor_copy(spread[:].rearrange("p c k (h r) -> p (c k h) r", r=HEAD),
                            small_s[:, ONE_HOT:ONE_HOT + 2 * HEADS].unsqueeze(2).to_broadcast([P, 2 * HEADS, HEAD])
                            ).then_inc(spread_set, 1)
            dve.wait_ge(q_made, 1)
            dve.tensor_tensor(q_s[:], q_ps, small_s[:, BQ:BQ + K].unsqueeze(2).to_broadcast([P, K, B]),
                              ALU.add).then_inc(q_biased, 1)
            dve.wait_ge(q_biased, 1)
            dve.scalar_tensor_tensor(
                q_heads[:].rearrange("p k b h -> p (k b) h"),
                q_s[:].rearrange("p k b -> p (k b)").unsqueeze(2).to_broadcast([P, K * B, HPK]), float(HEAD) ** -0.5,
                small_s[:, IN_HEAD:IN_HEAD + HPK].unsqueeze(1).to_broadcast([P, K * B, HPK]),
                ALU.mult, ALU.mult).then_inc(q_spread, 1)
            x_low(1)
            dve.wait_ge(a_made, 1)
            dve.wait_ge(a_zeroed, 1)
            dve.tensor_copy(a_st[:, :, :, 0:HEADS], a_ps).then_inc(a_high, 1)
            dve.wait_ge(a_high, 1)
            dve.tensor_tensor(a_st[:, :, :, 2 * Q:2 * Q + HEADS], a_ps, a_st[:, :, :, 0:HEADS].bitcast(F32),
                              ALU.subtract).then_inc(a_low, 1)
            for par in range(2):
                rows = slice((2 + par) * Q, (3 + par) * Q)
                dve.tensor_copy(score_bias[rows], cb_ps[rows, :, par, :]).then_inc(cb_set, 1)
            attention(0)
            dve.wait_ge(wo_high, 1)
            dve.tensor_tensor(wo_l[:], wo_s[:], wo_h[:].bitcast(F32), ALU.subtract).then_inc(wo_low, 1)
            context(0)
            attention(1)
            context(1)
            output(0)
            for c in range(2, CHUNKS):
                context(c)
                output(c - 1)
            output(CHUNKS - 1)

        @block.tensor
        def _(pe):
            def x_split(c):
                pe.wait_ge(xh_done, K * (c + 1))
                if c < DVE_XL:
                    pe.wait_ge(xl_done, K * (c + 1))
                else:
                    pe.wait_ge(xl_pool, c + 1 - DVE_XL)

            def value(c):
                for m in range(K):
                    if c > 0:
                        pe.wait_ge(v_kept, K * (c - 1) + m + 1)
                    for n, (w, x) in enumerate(((wv_h, x_h), (wv_l, x_h), (wv_h, x_l))):
                        if n == 0 and m == 0:
                            pe.wait_ge(xh_done, K * (c + 1))
                        if c == 0 and m == 0:
                            pe.wait_ge(wv_low if n == 1 else wv_high, 1)
                        if n == 2 and m == 0:
                            x_split(c)
                        for k in range(K):
                            last = pe.matmul(v_ps[m][:], w[:, k, m * P:(m + 1) * P], x[:, c, k, :],
                                             start=(n == 0 and k == 0), stop=(n == 2 and k == K - 1))
                    last.then_inc(v_made, 1)

            def scores(r):
                if r == 0:
                    pe.wait_ge(a_low, 1)
                else:
                    pe.wait_ge(s_sum, r)
                for j in range(BPC):
                    for par in range(2):
                        c = 2 * r + par
                        b = c * BPC + j
                        at = b * SLOT - par * Q
                        if j == 0:
                            x_split(c)
                        for x in (x_h, x_l):
                            for k in range(K):
                                last = pe.matmul(s_ps[:, j * T:(j + 1) * T], a_flat[:, k, at:at + P],
                                                 x[:, c, k, j * T:(j + 1) * T],
                                                 start=(par == 0 and x is x_h and k == 0),
                                                 stop=(par == 1 and x is x_l and k == K - 1))
                last.then_inc(s_made, 1)

            def expand(c):
                r = c // 2
                pe.wait_ge(attn_low, r + 1)
                if c == 0:
                    pe.wait_ge(spread_set, 1)
                for k in range(K):
                    if c > 0:
                        pe.wait_ge(ctx_made, K * (c - 1) + k + 1)
                    pe.matmul(e_ps[k][:], spread[:, c % 2, k, :], attn[:, r, :], start=True, stop=True
                              ).then_inc(e_made, 1)

            def project(c):
                for m in range(K):
                    if c > 0:
                        pe.wait_ge(y_made, K * (c - 1) + m + 1)
                    for n, (w, x) in enumerate(((wo_h, ctx_h), (wo_l, ctx_h), (wo_h, ctx_l))):
                        for k in range(K):
                            if m == 0 and n == 0:
                                pe.wait_ge(ctx_high, K * c + k + 1)
                            if m == 0 and n == 2:
                                pe.wait_ge(ctx_low, K * c + k + 1)
                            if m == 0 and c == 0 and n < 2:
                                pe.wait_ge((wo_high, wo_low)[n], 1)
                            last = pe.matmul(o_ps[m][:], w[:, k, m * P:(m + 1) * P], x[:, c, k, :],
                                             start=(n == 0 and k == 0), stop=(n == 2 and k == K - 1))
                    last.then_inc(o_made, 1)

            pe.wait_ge(zeros_set, 1)
            for _i in range(WARM):
                pe.matmul(o_ps[0][:], zeros[:, 0:P], zeros[:], start=True, stop=True)
            value(0)
            pe.wait_ge(wqc_in, 16)
            for m in range(K):
                for k in range(K):
                    last = pe.matmul(q_ps[:, m, :], wqc_s[:, k, m * P:(m + 1) * P], wqc_s[:, k, D:D + B],
                                     start=(k == 0), stop=(k == K - 1))
            last.then_inc(q_made, 1)
            value(1)
            pe.wait_ge(q_spread, 1)
            pe.wait_ge(wk_in, 16)
            for k in range(K):
                for j in range(K):
                    pe.matmul(a_ps[:, k, :, j * HPK:(j + 1) * HPK], wk_s[:, j, k * P:(k + 1) * P],
                                     q_heads[:, j], start=True, stop=True)
            pe.wait_ge(bk_set, 2 * K)
            for k in range(K):
                last = pe.matmul(p_ps[:, 16:16 + B], bk_heads[:, k, :], q_s[:, k, :], start=(k == 0), stop=(k == K - 1))
            last.then_inc(a_made, 1)
            scores(0)
            value(2)
            expand(0)
            scores(1)
            value(3)
            expand(1)
            project(0)
            for c in range(2, CHUNKS):
                expand(c)
                project(c - 1)
            project(CHUNKS - 1)


def kernel(x, cond_1024, L0_cond_Wq, L0_cond_bq, L0_cond_Wk, L0_cond_bk, L0_cond_Wv, L0_cond_bv, L0_cond_Wo,
           L0_cond_bo):
    import numpy as np
    import concourse.bacc as bacc
    from concourse.bass_utils import run_bass_kernel_spmd

    def by_feature(w):
        return np.asarray(w).T.reshape(K, P, -1).transpose(1, 0, 2)

    part = np.arange(P)
    one_hot = (part[:, None] % (2 * Q) == (np.arange(2)[:, None] * Q + np.arange(HEADS)).reshape(1, -1))
    in_head = (part[:, None] // HEAD == np.arange(HPK))
    arrays = {
        "x_t": np.asarray(x).reshape(CHUNKS, N, K, P).transpose(0, 3, 2, 1),
        "wq_cond": np.concatenate([by_feature(L0_cond_Wq), by_feature(cond_1024)], axis=2),
        "wk": np.asarray(L0_cond_Wk).reshape(K, P, D).transpose(1, 0, 2),
        "wv": by_feature(L0_cond_Wv),
        "wo": by_feature(L0_cond_Wo),
        "small": np.concatenate([np.asarray(b).reshape(K, P).T for b in (L0_cond_bq, L0_cond_bk, L0_cond_bv, L0_cond_bo)]
                                + [one_hot.astype(np.float32), in_head.astype(np.float32)], axis=1),
    }
    arrays = {name: np.ascontiguousarray(a) for name, a in arrays.items()}
    nc = bacc.Bacc("TRN2", target_bir_lowering=False, num_devices=1)
    args = [nc.dram_tensor(name, a.shape, F32, kind="ExternalInput").ap() for name, a in arrays.items()]
    y_t = nc.dram_tensor("y_t", (CHUNKS, K, P, N), F32, kind="ExternalOutput").ap()
    build(nc, *args, y_t)
    done = run_bass_kernel_spmd(nc, [arrays], core_ids=[0])
    y = done.results[0]["y_t"]
    return y.transpose(0, 3, 1, 2).reshape(B, T, D)
```

```python
from contextlib import ExitStack

import concourse.bass as bass
from concourse import mybir

F32 = mybir.dt.float32
F32R = mybir.dt.float32r
BF16 = mybir.dt.bfloat16
ALU = mybir.AluOpType
ACT = mybir.ActivationFunctionType

P = 128
B, T, D = 8, 256, 256
HEADS, HEAD = 16, 16
K = D // P
N = 512
CHUNKS = B * T // N
BPC = N // T
PAIRS = CHUNKS // 2
HPK = HEADS // K
Q = 32
SLOT = 160
WARM = 8

BQ, BK, BV, BO = 0, K, 2 * K, 3 * K
ONE_HOT = 4 * K
IN_HEAD = ONE_HOT + 2 * HEADS
SMALL = IN_HEAD + HPK


def build(nc, x_t, wq_cond, wk, wv, wo, small, y_t):
    with ExitStack() as ctx:
        def sb(name, shape, dt=F32):
            return ctx.enter_context(nc.sbuf_tensor(name, shape, dt))

        def bank(name):
            return ctx.enter_context(nc.psum_tensor(name, [P, N], F32))

        def sem(name):
            return ctx.enter_context(nc.semaphore(name))

        x_s = sb("x_s", [P, CHUNKS, K, N])
        x_h = sb("x_h", [P, CHUNKS, K, N], F32R)
        x_l = sb("x_l", [P, CHUNKS, K, N], F32R)
        v_s = sb("v_s", [P, CHUNKS, K, N])
        ctx_s = sb("ctx_s", [P, CHUNKS, K, N])
        ctx_h = sb("ctx_h", [P, CHUNKS, K, N], F32R)
        ctx_l = sb("ctx_l", [P, CHUNKS, K, N], F32R)
        y_s = sb("y_s", [P, CHUNKS, K, N])
        wqc_s = sb("wqc_s", [P, K, D + B])
        wk_s = sb("wk_s", [P, K, D])
        wv_s = sb("wv_s", [P, K, D])
        wv_h = sb("wv_h", [P, K, D], F32R)
        wv_l = sb("wv_l", [P, K, D], F32R)
        wo_s = sb("wo_s", [P, K, D])
        wo_h = sb("wo_h", [P, K, D], F32R)
        wo_l = sb("wo_l", [P, K, D], F32R)
        small_s = sb("small_s", [P, SMALL])
        q_s = sb("q_s", [P, K, B])
        q_heads = sb("q_heads", [P, K, B, HPK])
        bk_heads = sb("bk_heads", [P, K, P])
        a_st = sb("a_st", [P, K, B, SLOT], F32R)
        a_flat = a_st[:].rearrange("p k b s -> p k (b s)")
        score_bias = sb("score_bias", [P, PAIRS, BPC])
        low_s = sb("low_s", [P, N])
        sum_s = sb("sum_s", [P, N])
        clip_s = sb("clip_s", [P, N])
        attn = sb("attn", [P, PAIRS, N], F32R)
        spread = sb("spread", [P, 2, K, P], F32R)
        zeros_f = sb("zeros_f", [P, N // 2])
        zeros = zeros_f[:].bitcast(BF16)
        act_warm = sb("act_warm", [P, 1])

        acc = [[bank(f"acc{c}_{m}") for m in range(K)] for c in range(2)]
        e_ps = [bank(f"e_ps{k}") for k in range(K)]
        s_ps = bank("s_ps")
        p_ps = bank("p_ps")
        spread_ps = [e_ps, [s_ps, p_ps]]
        q_ps = p_ps[:, 0:K * B].rearrange("p (k b) -> p k b", k=K)
        cb_ps = p_ps[:, 16:16 + B].rearrange("p (r c b) -> p r c b", r=PAIRS, c=2)
        a_ps = p_ps[:, 256:512].rearrange("p (k b h) -> p k b h", k=K, b=B)

        x_in = [[sem(f"x_in{c}_{k}") for k in range(K)] for c in range(CHUNKS)]
        wv_in = [sem(f"wv_in{k}") for k in range(K)]
        wqc_in, wk_in, wo_in, small_in = (sem(s) for s in ("wqc_in", "wk_in", "wo_in", "small_in"))
        zeros_set = sem("zeros_set")
        a_zeroed = sem("a_zeroed")
        bk_zeroed = sem("bk_zeroed")
        bk_set = sem("bk_set")
        wv_high, wv_low, wo_high, wo_low = (sem(s) for s in ("wv_high", "wv_low", "wo_high", "wo_low"))
        xh_done = sem("xh_done")
        xl_done = sem("xl_done")
        xl_pool = sem("xl_pool")
        q_made, q_biased, q_spread = (sem(s) for s in ("q_made", "q_biased", "q_spread"))
        a_made, a_high, a_low = (sem(s) for s in ("a_made", "a_high", "a_low"))
        cb_set = sem("cb_set")
        spread_set = sem("spread_set")
        v_made, v_kept = sem("v_made"), sem("v_kept")
        s_made, s_low, s_sum, s_clip = (sem(s) for s in ("s_made", "s_low", "s_sum", "s_clip"))
        attn_high, attn_low = sem("attn_high"), sem("attn_low")
        e_made = sem("e_made")
        ctx_made, ctx_high, ctx_low = (sem(s) for s in ("ctx_made", "ctx_high", "ctx_low"))
        ctx_low_pool = sem("ctx_low_pool")
        o_made = sem("o_made")
        o_kept = sem("o_kept")
        y_dve, y_pool, y_out = sem("y_dve"), sem("y_pool"), sem("y_out")

        DVE_XL = 2
        whole = slice(0, N)
        halves = (slice(0, N // 2), slice(N // 2, N))

        def bias(at, k):
            return small_s[:, at + k:at + k + 1]

        block = ctx.enter_context(nc.Block())

        @block.sync
        def _(sp):
            sp.dma_start(x_s[:, 0, 0, :], x_t[0, :, 0, :]).then_inc(x_in[0][0], 16)
            for k in range(K):
                sp.dma_start(wv_s[:, k, :], wv[:, k, :]).then_inc(wv_in[k], 16)
            sp.dma_start(x_s[:, 0, 1, :], x_t[0, :, 1, :]).then_inc(x_in[0][1], 16)
            sp.dma_start(wqc_s[:], wq_cond).then_inc(wqc_in, 16)
            sp.dma_start(small_s[:], small).then_inc(small_in, 16)
            for k in range(K):
                sp.dma_start(x_s[:, 1, k, :], x_t[1, :, k, :]).then_inc(x_in[1][k], 16)
            sp.dma_start(wk_s[:], wk).then_inc(wk_in, 16)
            for c in range(2, CHUNKS):
                for k in range(K):
                    sp.dma_start(x_s[:, c, k, :], x_t[c, :, k, :]).then_inc(x_in[c][k], 16)
            sp.dma_start(wo_s[:], wo).then_inc(wo_in, 16)
            for done, n, c, m, cols in (
                    (y_pool, 1, 0, 0, whole), (y_pool, 2, 0, 1, whole), (y_dve, 1, 1, 0, whole), (y_pool, 3, 1, 1, whole),
                    (y_dve, 2, 2, 0, whole), (y_dve, 3, 2, 1, whole),
                    (y_dve, 4, 3, 0, whole), (y_dve, 5, 3, 1, halves[0]), (y_dve, 6, 3, 1, halves[1])):
                sp.wait_ge(done, n)
                sp.dma_start(y_t[c, m, :, cols], y_s[:, c, m, cols]).then_inc(y_out, 16)
            sp.wait_ge(y_out, 16 * (2 * CHUNKS + 1))

        @block.gpsimd
        def _(pool):
            pool.memset(a_st[:].bitcast(F32), 0.0).then_inc(a_zeroed, 1)
            pool.memset(bk_heads[:], 0.0).then_inc(bk_zeroed, 1)
            pool.wait_ge(bk_zeroed, 1)
            pool.wait_ge(small_in, 16)
            for k in range(K):
                for par in range(2):
                    at = 2 * Q + par * Q + k * HPK
                    pool.tensor_scalar(bk_heads[:, k, at:at + HPK], small_s[:, IN_HEAD:IN_HEAD + HPK],
                                       bias(BK, k), float(HEAD) ** -0.5, ALU.mult, ALU.mult).then_inc(bk_set, 1)
            for c in range(DVE_XL, CHUNKS):
                for k in range(K):
                    pool.wait_ge(xh_done, K * c + k + 1)
                    pool.tensor_tensor(x_l[:, c, k, :], x_s[:, c, k, :], x_h[:, c, k, :].bitcast(F32),
                                       ALU.subtract).then_inc(xl_pool, 1)
            pool.wait_ge(wo_high, 1)
            pool.tensor_tensor(wo_l[:], wo_s[:], wo_h[:].bitcast(F32), ALU.subtract).then_inc(wo_low, 1)
            pool.wait_ge(ctx_high, 2 * K)
            pool.tensor_tensor(ctx_l[:, 1, 1, :], ctx_s[:, 1, 1, :], ctx_h[:, 1, 1, :].bitcast(F32),
                               ALU.subtract).then_inc(ctx_low_pool, 1)
            for n, (c, m) in enumerate(((0, 0), (0, 1), (1, 1))):
                pool.wait_ge(o_kept, n + 1)
                pool.tensor_tensor(y_s[:, c, m, :], y_s[:, c, m, :], x_s[:, c, m, :], ALU.add).then_inc(y_pool, 1)

        @block.scalar
        def _(act):
            def x_high(c, k):
                act.wait_ge(x_in[c][k], 16)
                act.copy(x_h[:, c, k, :], x_s[:, c, k, :]).then_inc(xh_done, 1)

            def keep_v(c):
                for m in range(K):
                    act.wait_ge(v_made, K * c + m + 1)
                    act.activation(v_s[:, c, m, :], acc[c % 2][m][:], ACT.Identity, bias=bias(BV, m)
                                   ).then_inc(v_kept, 1)

            def score_low(r):
                act.wait_ge(s_made, r + 1)
                if r == 0:
                    act.wait_ge(cb_set, 2)
                else:
                    act.wait_ge(s_sum, r)
                for j in range(BPC):
                    act.activation(low_s[2 * Q:, j * T:(j + 1) * T], s_ps[2 * Q:, j * T:(j + 1) * T], ACT.Identity,
                                   bias=score_bias[2 * Q:, r, j:j + 1]).then_inc(s_low, 1)

            def ctx_round(c):
                for k in range(K):
                    act.wait_ge(ctx_made, K * c + k + 1)
                    act.copy(ctx_h[:, c, k, :], ctx_s[:, c, k, :]).then_inc(ctx_high, 1)

            def keep_output(c, m):
                act.wait_ge(o_made, K * c + m + 1)
                act.activation(y_s[:, c, m, :], acc[c % 2][m][:], ACT.Identity, bias=bias(BO, m)).then_inc(o_kept, 1)

            act.wait_ge(zeros_set, 1)
            act.activation(act_warm[:], zeros_f[:, 0:1], ACT.Identity)
            x_high(0, 0)
            for k in range(K):
                act.wait_ge(wv_in[k], 16)
                act.copy(wv_h[:, k, :], wv_s[:, k, :]).then_inc(wv_high, 1)
            x_high(0, 1)
            for k in range(K):
                x_high(1, k)
            act.wait_ge(small_in, 16)
            keep_v(0)
            for k in range(K):
                x_high(2, k)
            keep_v(1)
            for k in range(K):
                x_high(3, k)
            act.wait_ge(wo_in, 16)
            act.copy(wo_h[:], wo_s[:]).then_inc(wo_high, 1)
            score_low(0)
            keep_v(2)
            score_low(1)
            ctx_round(0)
            keep_v(3)
            ctx_round(1)
            keep_output(0, 0)
            keep_output(0, 1)
            ctx_round(2)
            keep_output(1, 1)
            ctx_round(3)

        @block.vector
        def _(dve):
            def x_low(c, k):
                dve.wait_ge(xh_done, K * c + k + 1)
                dve.tensor_tensor(x_l[:, c, k, :], x_s[:, c, k, :], x_h[:, c, k, :].bitcast(F32),
                                  ALU.subtract).then_inc(xl_done, 1)

            rows = slice(0, 2 * Q)

            def score_sum(r):
                dve.wait_ge(s_low, BPC * (r + 1))
                dve.tensor_tensor(sum_s[rows], s_ps[rows], low_s[2 * Q:], ALU.add).then_inc(s_sum, 1)

            def score_clip(r):
                dve.wait_ge(s_sum, r + 1)
                dve.tensor_scalar(clip_s[rows], sum_s[rows], 0.0, 1.0, ALU.max, ALU.min).then_inc(s_clip, 1)

            def score_high(r):
                dve.wait_ge(s_clip, r + 1)
                dve.tensor_copy(attn[rows, r, :], clip_s[rows]).then_inc(attn_high, 1)

            def score_rest(r):
                dve.wait_ge(attn_high, r + 1)
                dve.tensor_tensor(attn[2 * Q:, r, :], clip_s[rows], attn[rows, r, :].bitcast(F32),
                                  ALU.subtract).then_inc(attn_low, 1)

            def product(c):
                for k in range(K):
                    dve.wait_ge(e_made, K * c + k + 1)
                    dve.wait_ge(v_kept, K * c + k + 1)
                    dve.tensor_tensor(ctx_s[:, c, k, :], spread_ps[c % 2][k][:], v_s[:, c, k, :], ALU.mult
                                      ).then_inc(ctx_made, 1)

            def context_low(c, k):
                dve.wait_ge(ctx_high, K * c + k + 1)
                dve.tensor_tensor(ctx_l[:, c, k, :], ctx_s[:, c, k, :], ctx_h[:, c, k, :].bitcast(F32),
                                  ALU.subtract).then_inc(ctx_low, 1)

            def output(c, m, bank, part=0, cols=whole):
                dve.wait_ge(o_made, K * c + m + part + 1)
                dve.scalar_tensor_tensor(y_s[:, c, m, cols], bank[:, cols], bias(BO, m), x_s[:, c, m, cols],
                                         ALU.add, ALU.add).then_inc(y_dve, 1)

            dve.memset(zeros_f[:], 0.0).then_inc(zeros_set, 1)
            for k in range(K):
                dve.wait_ge(wv_high, k + 1)
                dve.tensor_tensor(wv_l[:, k, :], wv_s[:, k, :], wv_h[:, k, :].bitcast(F32), ALU.subtract
                                  ).then_inc(wv_low, 1)
                x_low(0, k)
            dve.wait_ge(small_in, 16)
            dve.tensor_copy(spread[:].rearrange("p c k (h r) -> p (c k h) r", r=HEAD),
                            small_s[:, ONE_HOT:ONE_HOT + 2 * HEADS].unsqueeze(2).to_broadcast([P, 2 * HEADS, HEAD])
                            ).then_inc(spread_set, 1)
            x_low(1, 0)
            dve.wait_ge(q_made, 1)
            dve.tensor_tensor(q_s[:], q_ps, small_s[:, BQ:BQ + K].unsqueeze(2).to_broadcast([P, K, B]),
                              ALU.add).then_inc(q_biased, 1)
            dve.wait_ge(q_biased, 1)
            dve.scalar_tensor_tensor(
                q_heads[:].rearrange("p k b h -> p (k b) h"),
                q_s[:].rearrange("p k b -> p (k b)").unsqueeze(2).to_broadcast([P, K * B, HPK]), float(HEAD) ** -0.5,
                small_s[:, IN_HEAD:IN_HEAD + HPK].unsqueeze(1).to_broadcast([P, K * B, HPK]),
                ALU.mult, ALU.mult).then_inc(q_spread, 1)
            x_low(1, 1)
            dve.wait_ge(a_made, 1)
            dve.wait_ge(a_zeroed, 1)
            dve.tensor_copy(a_st[:, :, :, 0:HEADS], a_ps).then_inc(a_high, 1)
            dve.wait_ge(a_high, 1)
            dve.tensor_tensor(a_st[:, :, :, 2 * Q:2 * Q + HEADS], a_ps, a_st[:, :, :, 0:HEADS].bitcast(F32),
                              ALU.subtract).then_inc(a_low, 1)
            for par in range(2):
                low_rows = slice((2 + par) * Q, (3 + par) * Q)
                dve.tensor_copy(score_bias[low_rows], cb_ps[low_rows, :, par, :]).then_inc(cb_set, 1)
            score_sum(0)
            score_clip(0)
            score_high(0)
            score_rest(0)
            product(0)
            score_sum(1)
            context_low(0, 0)
            score_clip(1)
            context_low(0, 1)
            score_high(1)
            product(1)
            score_rest(1)
            context_low(1, 0)
            product(2)
            context_low(2, 0)
            context_low(2, 1)
            product(3)
            output(1, 0, acc[1][0])
            context_low(3, 0)
            output(2, 0, acc[0][0])
            context_low(3, 1)
            output(2, 1, acc[0][1])
            output(3, 0, acc[1][0])
            for h in range(2):
                output(3, 1, e_ps[h], h, halves[h])

        @block.tensor
        def _(pe):
            def xl_ready(c):
                if c < DVE_XL:
                    pe.wait_ge(xl_done, K * (c + 1))
                else:
                    pe.wait_ge(xl_pool, K * (c + 1 - DVE_XL))

            def value_high(c, k):
                if c == 0:
                    pe.wait_ge(wv_high, k + 1)
                pe.wait_ge(xh_done, K * c + k + 1)
                for m in range(K):
                    pe.matmul(acc[c % 2][m][:], wv_h[:, k, m * P:(m + 1) * P], x_h[:, c, k, :],
                              start=(k == 0), stop=False)
                for m in range(K):
                    if c == 0:
                        pe.wait_ge(wv_low, k + 1)
                    pe.matmul(acc[c % 2][m][:], wv_l[:, k, m * P:(m + 1) * P], x_h[:, c, k, :],
                              start=False, stop=False)

            def value_low(c):
                xl_ready(c)
                for m in range(K):
                    for k in range(K):
                        last = pe.matmul(acc[c % 2][m][:], wv_h[:, k, m * P:(m + 1) * P], x_l[:, c, k, :],
                                         start=False, stop=(k == K - 1))
                    last.then_inc(v_made, 1)

            def query():
                pe.wait_ge(wqc_in, 16)
                for m in range(K):
                    for k in range(K):
                        last = pe.matmul(q_ps[:, m, :], wqc_s[:, k, m * P:(m + 1) * P], wqc_s[:, k, D:D + B],
                                         start=(k == 0), stop=(k == K - 1))
                last.then_inc(q_made, 1)

            def score_weights():
                pe.wait_ge(q_spread, 1)
                pe.wait_ge(wk_in, 16)
                for k in range(K):
                    for j in range(K):
                        pe.matmul(a_ps[:, k, :, j * HPK:(j + 1) * HPK], wk_s[:, j, k * P:(k + 1) * P],
                                  q_heads[:, j], start=True, stop=True)
                pe.wait_ge(bk_set, 2 * K)
                for k in range(K):
                    last = pe.matmul(p_ps[:, 16:16 + B], bk_heads[:, k, :], q_s[:, k, :],
                                     start=(k == 0), stop=(k == K - 1))
                last.then_inc(a_made, 1)

            def scores(r):
                if r == 0:
                    pe.wait_ge(a_low, 1)
                else:
                    pe.wait_ge(s_sum, r)
                for j in range(BPC):
                    for par in range(2):
                        c = 2 * r + par
                        b = c * BPC + j
                        at = b * SLOT - par * Q
                        if j == 0:
                            pe.wait_ge(xh_done, K * (c + 1))
                            xl_ready(c)
                        for x in (x_h, x_l):
                            for k in range(K):
                                last = pe.matmul(s_ps[:, j * T:(j + 1) * T], a_flat[:, k, at:at + P],
                                                 x[:, c, k, j * T:(j + 1) * T],
                                                 start=(par == 0 and x is x_h and k == 0),
                                                 stop=(par == 1 and x is x_l and k == K - 1))
                last.then_inc(s_made, 1)

            def expand(c):
                r = c // 2
                pe.wait_ge(attn_low, r + 1)
                if c == 0:
                    pe.wait_ge(spread_set, 1)
                elif c == 1:
                    pe.wait_ge(s_sum, PAIRS)
                    pe.wait_ge(cb_set, 2)
                else:
                    pe.wait_ge(ctx_made, K * (c - 1))
                for k in range(K):
                    pe.matmul(spread_ps[c % 2][k][:], spread[:, c % 2, k, :], attn[:, r, :], start=True, stop=True
                              ).then_inc(e_made, 1)

            def project(c):
                for k in range(K):
                    pe.wait_ge(ctx_high, K * c + k + 1)
                    for m in range(K):
                        for n, w in enumerate((wo_h, wo_l)):
                            if c == 0 and k == 0 and m == 0:
                                pe.wait_ge((wo_high, wo_low)[n], 1)
                            pe.matmul(acc[c % 2][m][:], w[:, k, m * P:(m + 1) * P], ctx_h[:, c, k, :],
                                      start=(k == 0 and n == 0), stop=False)
                pe.wait_ge(ctx_low, K + c)
                if c == 1:
                    pe.wait_ge(ctx_low_pool, 1)
                for m in range(K):
                    for k in range(K):
                        last = pe.matmul(acc[c % 2][m][:], wo_h[:, k, m * P:(m + 1) * P], ctx_l[:, c, k, :],
                                         start=False, stop=(k == K - 1))
                    last.then_inc(o_made, 1)

            def project_tile(c, m, bank, cols=whole):
                for n, (w, x) in enumerate(((wo_h, ctx_h), (wo_l, ctx_h), (wo_h, ctx_l))):
                    for k in range(K):
                        if m == 0 and n == 0:
                            pe.wait_ge(ctx_high, K * c + k + 1)
                        if m == 0 and n == 2:
                            pe.wait_ge(ctx_low, K * c + k)
                        last = pe.matmul(bank[:, cols], w[:, k, m * P:(m + 1) * P], x[:, c, k, cols],
                                         start=(n == 0 and k == 0), stop=(n == 2 and k == K - 1))
                last.then_inc(o_made, 1)

            pe.wait_ge(zeros_set, 1)
            for _i in range(WARM):
                pe.matmul(s_ps[:], zeros[:, 0:P], zeros, start=True, stop=True)
            for k in range(K):
                value_high(0, k)
            value_low(0)
            query()
            value_high(1, 0)
            score_weights()
            value_high(1, 1)
            value_low(1)
            scores(0)
            pe.wait_ge(v_kept, K)
            for k in range(K):
                value_high(2, k)
            value_low(2)
            scores(1)
            expand(0)
            pe.wait_ge(v_kept, 2 * K)
            for k in range(K):
                value_high(3, k)
            value_low(3)
            expand(1)
            pe.wait_ge(v_kept, 3 * K)
            project(0)
            expand(2)
            expand(3)
            pe.wait_ge(v_kept, 4 * K)
            project(1)
            pe.wait_ge(o_kept, 2)
            for m in range(K):
                project_tile(2, m, acc[0][m])
            pe.wait_ge(y_dve, 1)
            project_tile(3, 0, acc[1][0])
            pe.wait_ge(ctx_made, 3 * K)
            for h in range(2):
                project_tile(3, 1, e_ps[h], halves[h])


def kernel(x, cond_1024, L0_cond_Wq, L0_cond_bq, L0_cond_Wk, L0_cond_bk, L0_cond_Wv, L0_cond_bv, L0_cond_Wo,
           L0_cond_bo):
    import numpy as np
    import concourse.bacc as bacc
    from concourse.bass_utils import run_bass_kernel_spmd

    def by_feature(w):
        return np.asarray(w).T.reshape(K, P, -1).transpose(1, 0, 2)

    part = np.arange(P)
    one_hot = (part[:, None] % (2 * Q) == (np.arange(2)[:, None] * Q + np.arange(HEADS)).reshape(1, -1))
    in_head = (part[:, None] // HEAD == np.arange(HPK))
    arrays = {
        "x_t": np.asarray(x).reshape(CHUNKS, N, K, P).transpose(0, 3, 2, 1),
        "wq_cond": np.concatenate([by_feature(L0_cond_Wq), by_feature(cond_1024)], axis=2),
        "wk": np.asarray(L0_cond_Wk).reshape(K, P, D).transpose(1, 0, 2),
        "wv": by_feature(L0_cond_Wv),
        "wo": by_feature(L0_cond_Wo),
        "small": np.concatenate([np.asarray(b).reshape(K, P).T for b in (L0_cond_bq, L0_cond_bk, L0_cond_bv, L0_cond_bo)]
                                + [one_hot.astype(np.float32), in_head.astype(np.float32)], axis=1),
    }
    arrays = {name: np.ascontiguousarray(a) for name, a in arrays.items()}
    nc = bacc.Bacc("TRN2", target_bir_lowering=False, num_devices=1)
    args = [nc.dram_tensor(name, a.shape, F32, kind="ExternalInput").ap() for name, a in arrays.items()]
    y_t = nc.dram_tensor("y_t", (CHUNKS, K, P, N), F32, kind="ExternalOutput").ap()
    build(nc, *args, y_t)
    done = run_bass_kernel_spmd(nc, [arrays], core_ids=[0])
    y = done.results[0]["y_t"]
    return y.transpose(0, 3, 1, 2).reshape(B, T, D)
```
